# Optimizing a Trainium2 kernel written in Bass

```python
import numpy as np
import jax
import jax.numpy as jnp

def _softmax(x, axis=-1):
    return jax.nn.softmax(x, axis=axis)

def _gelu(x):
    return jax.nn.gelu(x, approximate=True)

def _silu(x):
    return jax.nn.silu(x)

def _sigmoid(x):
    return jax.nn.sigmoid(x)

def _layernorm(x, axis=-1, eps=1e-05):
    m = jnp.mean(x, axis=axis, keepdims=True)
    v = jnp.var(x, axis=axis, keepdims=True)
    return (x - m) / jnp.sqrt(v + eps)

def _scatter_add(tgt, idx, src, axis=0):
    return tgt.at[idx].add(src)

def _segment_sum(src, seg, n):
    return jax.ops.segment_sum(src, seg, n)
kernel_name = 'mk_dlrm_tower_d1_rec_r8_aaba21'

def setup_inputs(seed: int=0):
    np.random.seed(seed)
    _w = jnp.asarray

    def _rec_inputs():
        import jax
        import jax.numpy as jnp
        _tk = jax.random.key(seed)
        ids = jnp.stack([jax.random.randint(jax.random.fold_in(_tk, 200 + f), (2048,), 0, v, jnp.int32) for f, v in enumerate([125000, 1000, 1250, 1250, 12500, 1250, 12500, 1000, 12500, 12500, 1000, 12500, 1250, 12500, 12500, 12500, 1250, 1000, 1250, 1250, 1000, 1250, 1000, 1250, 1250, 1250])], axis=1)
        tbl_0 = 0.05 * jax.random.normal(jax.random.fold_in(_tk, 500 + 0), (125000, 128), jnp.float32)
        tbl_1 = 0.05 * jax.random.normal(jax.random.fold_in(_tk, 500 + 1), (1000, 128), jnp.float32)
        tbl_2 = 0.05 * jax.random.normal(jax.random.fold_in(_tk, 500 + 2), (1250, 128), jnp.float32)
        tbl_3 = 0.05 * jax.random.normal(jax.random.fold_in(_tk, 500 + 3), (1250, 128), jnp.float32)
        tbl_4 = 0.05 * jax.random.normal(jax.random.fold_in(_tk, 500 + 4), (12500, 128), jnp.float32)
        tbl_5 = 0.05 * jax.random.normal(jax.random.fold_in(_tk, 500 + 5), (1250, 128), jnp.float32)
        tbl_6 = 0.05 * jax.random.normal(jax.random.fold_in(_tk, 500 + 6), (12500, 128), jnp.float32)
        tbl_7 = 0.05 * jax.random.normal(jax.random.fold_in(_tk, 500 + 7), (1000, 128), jnp.float32)
        tbl_8 = 0.05 * jax.random.normal(jax.random.fold_in(_tk, 500 + 8), (12500, 128), jnp.float32)
        tbl_9 = 0.05 * jax.random.normal(jax.random.fold_in(_tk, 500 + 9), (12500, 128), jnp.float32)
        tbl_10 = 0.05 * jax.random.normal(jax.random.fold_in(_tk, 500 + 10), (1000, 128), jnp.float32)
        tbl_11 = 0.05 * jax.random.normal(jax.random.fold_in(_tk, 500 + 11), (12500, 128), jnp.float32)
        tbl_12 = 0.05 * jax.random.normal(jax.random.fold_in(_tk, 500 + 12), (1250, 128), jnp.float32)
        tbl_13 = 0.05 * jax.random.normal(jax.random.fold_in(_tk, 500 + 13), (12500, 128), jnp.float32)
        tbl_14 = 0.05 * jax.random.normal(jax.random.fold_in(_tk, 500 + 14), (12500, 128), jnp.float32)
        tbl_15 = 0.05 * jax.random.normal(jax.random.fold_in(_tk, 500 + 15), (12500, 128), jnp.float32)
        tbl_16 = 0.05 * jax.random.normal(jax.random.fold_in(_tk, 500 + 16), (1250, 128), jnp.float32)
        tbl_17 = 0.05 * jax.random.normal(jax.random.fold_in(_tk, 500 + 17), (1000, 128), jnp.float32)
        tbl_18 = 0.05 * jax.random.normal(jax.random.fold_in(_tk, 500 + 18), (1250, 128), jnp.float32)
        tbl_19 = 0.05 * jax.random.normal(jax.random.fold_in(_tk, 500 + 19), (1250, 128), jnp.float32)
        tbl_20 = 0.05 * jax.random.normal(jax.random.fold_in(_tk, 500 + 20), (1000, 128), jnp.float32)
        tbl_21 = 0.05 * jax.random.normal(jax.random.fold_in(_tk, 500 + 21), (1250, 128), jnp.float32)
        tbl_22 = 0.05 * jax.random.normal(jax.random.fold_in(_tk, 500 + 22), (1000, 128), jnp.float32)
        tbl_23 = 0.05 * jax.random.normal(jax.random.fold_in(_tk, 500 + 23), (1250, 128), jnp.float32)
        tbl_24 = 0.05 * jax.random.normal(jax.random.fold_in(_tk, 500 + 24), (1250, 128), jnp.float32)
        tbl_25 = 0.05 * jax.random.normal(jax.random.fold_in(_tk, 500 + 25), (1250, 128), jnp.float32)
        _rk = jax.random.fold_in(_tk, 7)
        r_dense_features = -0.000520686 + 1.00062 * jax.random.normal(jax.random.fold_in(_rk, 101), (2048, 128), jnp.float32)
        W_top1 = 0.0405887 * jax.random.normal(jax.random.fold_in(_tk, 801), (607, 512), jnp.float32)
        W_top2 = 0.0441942 * jax.random.normal(jax.random.fold_in(_tk, 802), (512, 256), jnp.float32)
        W_top3 = 0.0625 * jax.random.normal(jax.random.fold_in(_tk, 803), (256, 1), jnp.float32)
        b_top1 = jnp.zeros((512,), jnp.float32)
        b_top2 = jnp.zeros((256,), jnp.float32)
        return (r_dense_features, ids, tbl_0, tbl_1, tbl_2, tbl_3, tbl_4, tbl_5, tbl_6, tbl_7, tbl_8, tbl_9, tbl_10, tbl_11, tbl_12, tbl_13, tbl_14, tbl_15, tbl_16, tbl_17, tbl_18, tbl_19, tbl_20, tbl_21, tbl_22, tbl_23, tbl_24, tbl_25, W_top1, b_top1, W_top2, b_top2, W_top3)
    r_dense_features, ids, tbl_0, tbl_1, tbl_2, tbl_3, tbl_4, tbl_5, tbl_6, tbl_7, tbl_8, tbl_9, tbl_10, tbl_11, tbl_12, tbl_13, tbl_14, tbl_15, tbl_16, tbl_17, tbl_18, tbl_19, tbl_20, tbl_21, tbl_22, tbl_23, tbl_24, tbl_25, W_top1, b_top1, W_top2, b_top2, W_top3 = _rec_inputs()

    def _L0_rec_setup():
        import jax, jax.numpy as jnp
        import numpy as np
        B, F, D = (2048, 26, 128)
        key = jax.random.key(seed)
        k1, k2 = jax.random.split(key)
        dense_features = jax.random.normal(k1, (B, D), dtype=jnp.float32)
        sparse_values = jax.random.normal(k2, (B, F, D), dtype=jnp.float32)
        return {'dense_features': dense_features, 'sparse_values': sparse_values}
    _L0_rec_all = _L0_rec_setup()
    _L0_rec_in = {k: v for k, v in _L0_rec_all.items() if k in ()}
    del _L0_rec_all
    return {'r_dense_features': r_dense_features, 'ids': ids, 'tbl_0': tbl_0, 'tbl_1': tbl_1, 'tbl_2': tbl_2, 'tbl_3': tbl_3, 'tbl_4': tbl_4, 'tbl_5': tbl_5, 'tbl_6': tbl_6, 'tbl_7': tbl_7, 'tbl_8': tbl_8, 'tbl_9': tbl_9, 'tbl_10': tbl_10, 'tbl_11': tbl_11, 'tbl_12': tbl_12, 'tbl_13': tbl_13, 'tbl_14': tbl_14, 'tbl_15': tbl_15, 'tbl_16': tbl_16, 'tbl_17': tbl_17, 'tbl_18': tbl_18, 'tbl_19': tbl_19, 'tbl_20': tbl_20, 'tbl_21': tbl_21, 'tbl_22': tbl_22, 'tbl_23': tbl_23, 'tbl_24': tbl_24, 'tbl_25': tbl_25, 'W_top1': W_top1, 'b_top1': b_top1, 'W_top2': W_top2, 'b_top2': b_top2, 'W_top3': W_top3}

def reference(r_dense_features, ids, tbl_0, tbl_1, tbl_2, tbl_3, tbl_4, tbl_5, tbl_6, tbl_7, tbl_8, tbl_9, tbl_10, tbl_11, tbl_12, tbl_13, tbl_14, tbl_15, tbl_16, tbl_17, tbl_18, tbl_19, tbl_20, tbl_21, tbl_22, tbl_23, tbl_24, tbl_25, W_top1, b_top1, W_top2, b_top2, W_top3):
    import jax
    import jax.numpy as jnp

    def _L0_rec_ref(dense_features, sparse_values):
        import jax, jax.numpy as jnp
        import numpy as np
        B, F, D = (2048, 26, 128)
        sd = jnp.einsum('bfd,bd->bf', sparse_values, dense_features)
        ss = jnp.einsum('bfd,bgd->bfg', sparse_values, sparse_values)
        iu, ju = jnp.triu_indices(F, k=1)
        pairs = ss[:, iu, ju]
        return jnp.concatenate([dense_features, sd, pairs], axis=1)
    e = jnp.stack([tbl_0[ids[:, 0]], tbl_1[ids[:, 1]], tbl_2[ids[:, 2]], tbl_3[ids[:, 3]], tbl_4[ids[:, 4]], tbl_5[ids[:, 5]], tbl_6[ids[:, 6]], tbl_7[ids[:, 7]], tbl_8[ids[:, 8]], tbl_9[ids[:, 9]], tbl_10[ids[:, 10]], tbl_11[ids[:, 11]], tbl_12[ids[:, 12]], tbl_13[ids[:, 13]], tbl_14[ids[:, 14]], tbl_15[ids[:, 15]], tbl_16[ids[:, 16]], tbl_17[ids[:, 17]], tbl_18[ids[:, 18]], tbl_19[ids[:, 19]], tbl_20[ids[:, 20]], tbl_21[ids[:, 21]], tbl_22[ids[:, 22]], tbl_23[ids[:, 23]], tbl_24[ids[:, 24]], tbl_25[ids[:, 25]]], axis=1)
    z = _L0_rec_ref(r_dense_features, e)
    z = z.reshape(z.shape[0], -1)
    h = jnp.concatenate([z, r_dense_features], axis=1)
    h = jnp.maximum(h @ W_top1 + b_top1, 0.0)
    h = jnp.maximum(h @ W_top2 + b_top2, 0.0)
    y = h @ W_top3
    return y

_drawn_inputs = setup_inputs


def setup_inputs(seed=0):
    import zlib

    import numpy as np

    out = dict(_drawn_inputs(seed))
    spreads = {'b_top1': (0.0, 0.1), 'b_top2': (0.0, 0.1)}
    factors = {}
    for name, (base, spread) in spreads.items():
        noise = np.random.default_rng([zlib.crc32(name.encode()), seed]).standard_normal(out[name].shape)
        drawn = base * np.exp(spread * noise) if base else spread * noise
        out[name] = jnp.asarray(drawn.astype(out[name].dtype))
    for name, factor in factors.items():
        out[name] = (out[name] * factor).astype(out[name].dtype)
    return out
```

```python
from contextlib import ExitStack

import numpy as np

import concourse.bass as bass
from concourse import mybir

F32 = mybir.dt.float32
I32 = mybir.dt.int32
ALU = mybir.AluOpType
ACT = mybir.ActivationFunctionType

BATCH = 2048
D = 128
NF = 26
NV = NF + 1
SLOT = 32
P = 128
TILES = BATCH // P
PAIRS_OF_TILES = TILES // 2
H1, H2 = 512, 256
M1, M2 = H1 // P, H2 // P

SHIFTS = NV // 2
NPAIR = NV * SHIFTS
KT = 3
ROWS = NV // KT
KP = ROWS * SHIFTS
WIDE = NV + SHIFTS

GROUP = 4
NG = (NV + GROUP - 1) // GROUP
GROUPS = [list(range(g * GROUP, min(g * GROUP + GROUP, NV))) for g in range(NG)]
GATHERS = [sum(v < NF for v in vs) for vs in GROUPS]
TBANKS = 3
GRAM_BANKS = 2
QUADS = 4
PER_QUAD = P // QUADS
PER_BANK = PER_QUAD // GRAM_BANKS


def pair_rows():
    rows = []
    for i in range(NV):
        for t in range(1, SHIFTS + 1):
            a, b = sorted((i, (i + t) % NV))
            if b == NF:
                rows.append(D + a)
            else:
                rows.append(D + NF + a * NF - a * (a + 1) // 2 + b - a - 1)
    return rows


def build(nc, dense, ids, tables, w1_pairs, w1_dense, b1, w2, b2, w3, out):
    with ExitStack() as ctx:
        def sb(name, shape, dt=F32):
            return ctx.enter_context(nc.sbuf_tensor(name, shape, dt))

        def sem(name):
            return ctx.enter_context(nc.semaphore(name))

        ident = sb("ident", [P, P])
        w1p = sb("w1p", [KP, KT, H1])
        w1d = sb("w1d", [D, 2, H1])
        w1x = sb("w1x", [D, H1])
        w2s = sb("w2s", [P, M1, H2])
        w3s = sb("w3s", [P, M2])
        b1s = sb("b1s", [P, M1])
        b2s = sb("b2s", [P, M2])
        idx = [sb(f"idx{q}", [P, NF], I32) for q in range(2)]
        rows = [sb(f"rows{q}", [P, NV, D]) for q in range(2)]
        emb = [sb(f"emb{q}", [D, P, SLOT]) for q in range(2)]
        xT = [sb(f"xT{q}", [D, P]) for q in range(2)]
        gram = sb("gram", [P, SLOT, WIDE])
        packed = sb("packed", [P, NPAIR])
        feat = sb("feat", [KP, KT, P])
        h1 = sb("h1", [P, M1, P])
        h2 = sb("h2", [P, M2, P])
        y_sb = sb("y_sb", [1, P])

        psT = [ctx.enter_context(nc.psum_tensor(f"psT{b}", [P, GROUP, P], F32)) for b in range(TBANKS)]
        psG = ctx.enter_context(nc.psum_tensor("psG", [P, GRAM_BANKS, 512], F32))
        psF = ctx.enter_context(nc.psum_tensor("psF", [P, 4, P], F32))
        psH1 = ctx.enter_context(nc.psum_tensor("psH1", [P, M1, P], F32))
        psH2 = ctx.enter_context(nc.psum_tensor("psH2", [P, 4, P], F32))
        psY = psH2[0:1, M2, :]

        consts_loaded = sem("consts_loaded")
        ident_zeroed = sem("ident_zeroed")
        ident_ready = sem("ident_ready")
        pads_zeroed = sem("pads_zeroed")
        w1x_ready = sem("w1x_ready")
        ids_loaded = [sem(f"ids_loaded{q}") for q in range(2)]
        dense_loaded = [sem(f"dense_loaded{q}") for q in range(2)]
        gathered = [[sem(f"gathered{q}_{g}") for g in range(NG)] for q in range(2)]
        transposed = sem("transposed")
        emb_by_act = sem("emb_by_act")
        emb_by_dve = sem("emb_by_dve")
        gram_done = sem("gram_done")
        gram_turned = sem("gram_turned")
        packed_ready = sem("packed_ready")
        feat_turned = sem("feat_turned")
        feat_ready = sem("feat_ready")
        l1_done = sem("l1_done")
        h1_ready = sem("h1_ready")
        l2_done = sem("l2_done")
        h2_ready = sem("h2_ready")
        l3_done = sem("l3_done")
        y_copied = sem("y_copied")
        y_stored = sem("y_stored")
        N_CONSTS = 6

        def moved(pair, n):
            return (emb_by_dve if n % 2 else emb_by_act), NG * pair + (n // 2 + 1)

        def bank_before(pair, n):
            if n >= TBANKS:
                return pair, n - TBANKS
            return pair - 1, max(m for m in range(2 * NG) if m % TBANKS == n)

        def before(pair, q):
            return (pair, 0) if q else (pair - 1, 1)

        block = ctx.enter_context(nc.Block())

        @block.sync
        def _(sp):
            def load(pair, q, fresh):
                if not fresh:
                    sp.wait_ge(transposed, 2 * NG * pair + (NG * q - NG))
                at = bass.ds((2 * pair + q) * P, P)
                sp.dma_start(idx[q][:, :], ids[at, :]).then_inc(ids_loaded[q], 16)
                sp.dma_start(rows[q][:, NF, :], dense[at, :]).then_inc(dense_loaded[q], 16)

            load(0, 0, True)
            load(0, 1, True)
            with sp.Fori(1, PAIRS_OF_TILES) as pair:
                load(pair, 0, False)
                load(pair, 1, False)

        @block.gpsimd
        def _(pool):
            nc.gpsimd.memset(ident[:, :], 0.0).then_inc(ident_zeroed, 1)
            pool.wait_ge(ident_zeroed, 1)
            nc.gpsimd.affine_select(out=ident[:, :], in_=ident[:, :], compare_op=ALU.not_equal, fill=1.0,
                                    base=0, pattern=[[-1, P]], channel_multiplier=1).then_inc(ident_ready, 1)

            freed = pool.alloc_register("freed")

            def gather(pair, q, fresh):
                pool.wait_ge(ids_loaded[q], 16 * pair + 16)
                for g, vectors in enumerate(GROUPS):
                    if not fresh:
                        pool.wait_ge(transposed, freed)
                        pool.reg_add(freed, freed, 1)
                    for v in vectors:
                        if v < NF:
                            pool.indirect_dma_start(
                                out=rows[q][:, v, :], out_offset=None, in_=tables[v],
                                in_offset=bass.IndirectOffsetOnAxis(ap=idx[q][:, v:v + 1], axis=0),
                            ).then_inc(gathered[q][g], 16)

            gather(0, 0, True)
            gather(0, 1, True)
            pool.reg_mov(freed, 1)
            with pool.Fori(1, PAIRS_OF_TILES) as pair:
                gather(pair, 0, False)
                gather(pair, 1, False)

        def move_group(eng, copy, pair, q, g, fresh):
            n = NG * q + g
            eng.wait_ge(transposed, 2 * NG * pair + (n + 1))
            if not fresh:
                eng.wait_ge(gram_done, 2 * pair + (q - 1))
                if g == NG - 1:
                    eng.wait_ge(l1_done, 2 * pair + (q - 1))
            vectors = GROUPS[g]
            last = copy(emb[q][:, :, vectors[0]:vectors[-1] + 1],
                        psT[n % TBANKS][:, 0:len(vectors), :].rearrange("d v b -> d b v"))
            if g == NG - 1:
                last = copy(xT[q][:, :], psT[n % TBANKS][:, NF - vectors[0], :])
            return last

        @block.scalar
        def _(act):
            act.dma_start(w1p[:, :, :], w1_pairs).then_inc(consts_loaded, 16)
            act.dma_start(w1d[:, :, :], w1_dense).then_inc(consts_loaded, 16)
            act.dma_start(b1s[:, :], b1).then_inc(consts_loaded, 16)
            act.dma_start(w2s[:, :, :], w2).then_inc(consts_loaded, 16)
            act.dma_start(b2s[:, :], b2).then_inc(consts_loaded, 16)
            act.dma_start(w3s[:, :], w3).then_inc(consts_loaded, 16)

            def move(pair, q, fresh):
                for g in range(NG):
                    if (NG * q + g) % 2 == 0:
                        move_group(act, nc.scalar.copy, pair, q, g, fresh).then_inc(emb_by_act, 1)

            def head(pair, q, fresh):
                act.wait_ge(l1_done, 2 * pair + (q + 1))
                act.wait_ge(l2_done, 2 * pair + q)
                for m in range(M1):
                    nc.scalar.activation(h1[:, m, :], psH1[:, m, :], ACT.Relu,
                                         bias=b1s[:, m:m + 1]).then_inc(h1_ready, 1)
                act.wait_ge(l2_done, 2 * pair + (q + 1))
                act.wait_ge(l3_done, 2 * pair + q)
                for m in range(M2):
                    nc.scalar.activation(h2[:, m, :], psH2[:, m, :], ACT.Relu,
                                         bias=b2s[:, m:m + 1]).then_inc(h2_ready, 1)
                act.wait_ge(l3_done, 2 * pair + (q + 1))
                if not fresh:
                    act.wait_ge(y_stored, 32 * pair + 16 * q)
                nc.scalar.copy(y_sb[:, :], psY).then_inc(y_copied, 1)
                act.wait_ge(y_copied, 2 * pair + (q + 1))
                act.dma_start(out[:, bass.ds((2 * pair + q) * P, P)], y_sb[:, :]).then_inc(y_stored, 16)

            move(0, 0, True)
            act.wait_ge(consts_loaded, 16 * N_CONSTS)
            move(0, 1, True)
            head(0, 0, True)
            with act.Fori(1, PAIRS_OF_TILES) as pair:
                move(pair, 0, False)
                head(pair - 1, 1, False)
                move(pair, 1, False)
                head(pair, 0, False)
            head(PAIRS_OF_TILES - 1, 1, False)
            act.wait_ge(y_stored, 16 * TILES)

        @block.vector
        def _(dve):
            for q in range(2):
                nc.vector.memset(emb[q][:, :, NV:SLOT], 0.0).then_inc(pads_zeroed, 1)
            dve.wait_ge(consts_loaded, 16 * N_CONSTS)
            nc.vector.tensor_tensor(w1x[:, :], w1d[:, 0, :], w1d[:, 1, :], ALU.add).then_inc(w1x_ready, 1)

            def move(pair, q, gs, fresh):
                for g in gs:
                    if (NG * q + g) % 2 == 1:
                        move_group(dve, nc.vector.tensor_copy, pair, q, g, fresh).then_inc(emb_by_dve, 1)

            def take_features(pair, q):
                dve.wait_ge(feat_turned, 2 * pair + (q + 1))
                dve.wait_ge(l1_done, 2 * pair + q)
                nc.vector.tensor_copy(feat[:, :, :], psF[0:KP, 0:KT, :]).then_inc(feat_ready, 1)

            def turn_gram(pair, q):
                dve.wait_ge(gram_done, 2 * pair + (q + 1))
                dve.wait_ge(packed_ready, 2 * pair + q)
                for lo, n in ((0, NV), (NV, SHIFTS)):
                    src = psG[:, :, 0:PER_BANK * NV].rearrange("p k (g j) -> p j k g", j=NV)[:, 0:n, :, :]
                    dst = gram[:, :, lo:lo + n].rearrange("p i j -> p j i")
                    nc.vector.transpose(dst, src).then_inc(gram_turned, 1)
                dve.wait_ge(gram_turned, 4 * pair + (2 * q + 2))
                dve.wait_ge(feat_turned, 2 * pair + q)
                src = gram[:, :, :].rearrange("p i j -> p (i j)")[:, 1:NV * (WIDE + 1) + 1]
                src = src.rearrange("p (i j) -> p i j", j=WIDE + 1)[:, :, 0:SHIFTS]
                dst = packed[:, :].rearrange("p (i t) -> p i t", t=SHIFTS)
                nc.vector.tensor_copy(dst, src).then_inc(packed_ready, 1)

            move(0, 0, range(NG), True)
            turn_gram(0, 0)

            def step(pair, q, fresh):
                move(pair, q, range(0, 4), fresh)
                take_features(*before(pair, q))
                move(pair, q, range(4, NG), fresh)
                turn_gram(pair, q)

            step(0, 1, True)
            with dve.Fori(1, PAIRS_OF_TILES) as pair:
                step(pair, 0, False)
                step(pair, 1, False)
            take_features(PAIRS_OF_TILES - 1, 1)

        @block.tensor
        def _(pe):
            def turn_rows(pair, q, gs, fresh):
                for g in gs:
                    n = NG * q + g
                    if GATHERS[g]:
                        pe.wait_ge(gathered[q][g], (16 * GATHERS[g]) * pair + 16 * GATHERS[g])
                    if NF in GROUPS[g]:
                        pe.wait_ge(dense_loaded[q], 16 * pair + 16)
                    if not fresh or n >= TBANKS:
                        pe.wait_ge(*moved(*bank_before(pair, n)))
                    for k, v in enumerate(GROUPS[g]):
                        last = nc.tensor.transpose(psT[n % TBANKS][:, k, :], rows[q][:, v, :], ident[:, :])
                    last.then_inc(transposed, 1)

            def products(pair, q, bank):
                if bank == 0:
                    pe.wait_ge(*moved(pair, NG * q + NG - 1))
                    pe.wait_ge(*moved(pair, NG * q + NG - 2))
                    pe.wait_ge(gram_turned, 4 * pair + 2 * q)
                for g in range(PER_BANK):
                    for c in range(QUADS):
                        b = c * PER_QUAD + bank * PER_BANK + g
                        last = nc.tensor.matmul(
                            psG[c * SLOT:(c + 1) * SLOT, bank, g * NV:(g + 1) * NV],
                            emb[q][:, b, :], emb[q][:, b, 0:NV], start=True, stop=True)
                if bank == GRAM_BANKS - 1:
                    last.then_inc(gram_done, 1)

            def turn_features(pair, q):
                pe.wait_ge(packed_ready, 2 * pair + (q + 1))
                pe.wait_ge(feat_ready, 2 * pair + q)
                for k in range(KT):
                    last = nc.tensor.transpose(psF[0:KP, k, :], packed[:, k * KP:(k + 1) * KP], ident[:, :])
                last.then_inc(feat_turned, 1)

            def layer1(pair, q):
                pe.wait_ge(feat_ready, 2 * pair + (q + 1))
                pe.wait_ge(h1_ready, (2 * M1) * pair + M1 * q)
                for m in range(M1):
                    cols = slice(m * P, (m + 1) * P)
                    nc.tensor.matmul(psH1[:, m, :], w1x[:, cols], xT[q][:, :], start=True, stop=False)
                    for k in range(KT):
                        last = nc.tensor.matmul(psH1[:, m, :], w1p[:, k, cols], feat[:, k, :],
                                                start=False, stop=(k == KT - 1))
                last.then_inc(l1_done, 1)

            def layer2(pair, q):
                pe.wait_ge(h1_ready, (2 * M1) * pair + (M1 * q + M1))
                pe.wait_ge(y_copied, 2 * pair + q)
                for m in range(M2):
                    for k in range(M1):
                        last = nc.tensor.matmul(psH2[:, m, :], w2s[:, k, m * P:(m + 1) * P], h1[:, k, :],
                                                start=(k == 0), stop=(k == M1 - 1))
                last.then_inc(l2_done, 1)

            def layer3(pair, q):
                pe.wait_ge(h2_ready, (2 * M2) * pair + (M2 * q + M2))
                for k in range(M2):
                    last = nc.tensor.matmul(psY, w3s[:, k:k + 1], h2[:, k, :],
                                            start=(k == 0), stop=(k == M2 - 1))
                last.then_inc(l3_done, 1)

            pe.wait_ge(ident_ready, 1)
            turn_rows(0, 0, range(NG), True)
            pe.wait_ge(pads_zeroed, 2)
            products(0, 0, 0)
            products(0, 0, 1)
            pe.wait_ge(consts_loaded, 16 * N_CONSTS)
            pe.wait_ge(w1x_ready, 1)

            def step(pair, q, fresh):
                done = before(pair, q)
                turn_rows(pair, q, range(0, 4), fresh)
                turn_features(*done)
                turn_rows(pair, q, range(4, NG), fresh)
                layer1(*done)
                products(pair, q, 0)
                layer2(*done)
                products(pair, q, 1)
                layer3(*done)

            step(0, 1, True)
            with pe.Fori(1, PAIRS_OF_TILES) as pair:
                step(pair, 0, False)
                step(pair, 1, False)
            final = (PAIRS_OF_TILES - 1, 1)
            turn_features(*final)
            layer1(*final)
            layer2(*final)
            layer3(*final)


def kernel(**inputs):
    from concourse import bacc
    from concourse.bass_utils import run_bass_kernel_spmd

    w1 = np.asarray(inputs["W_top1"])
    w2 = np.asarray(inputs["W_top2"])
    w3 = np.asarray(inputs["W_top3"])
    arrays = {
        "dense": np.asarray(inputs["r_dense_features"]),
        "ids": np.asarray(inputs["ids"]),
        "w1_pairs": w1[pair_rows()].reshape(KT, KP, H1).transpose(1, 0, 2),
        "w1_dense": np.stack([w1[:D], w1[-D:]], axis=1),
        "b1": np.asarray(inputs["b_top1"]).reshape(M1, P).T,
        "w2": w2.reshape(M1, P, H2).transpose(1, 0, 2),
        "b2": np.asarray(inputs["b_top2"]).reshape(M2, P).T,
        "w3": w3.reshape(M2, P).T,
    }
    for f in range(NF):
        arrays[f"tbl_{f}"] = np.asarray(inputs[f"tbl_{f}"])
    arrays = {k: np.ascontiguousarray(v) for k, v in arrays.items()}

    nc = bacc.Bacc("TRN2", target_bir_lowering=False, num_devices=1)
    arg = {k: nc.dram_tensor(k, v.shape, mybir.dt.from_np(v.dtype), kind="ExternalInput").ap()
           for k, v in arrays.items()}
    out = nc.dram_tensor("y", [1, BATCH], F32, kind="ExternalOutput").ap()
    build(nc, arg["dense"], arg["ids"], [arg[f"tbl_{f}"] for f in range(NF)], arg["w1_pairs"],
          arg["w1_dense"], arg["b1"], arg["w2"], arg["b2"], arg["w3"], out)
    r = run_bass_kernel_spmd(nc, [arrays], core_ids=[0])
    return r.results[0]["y"].reshape(BATCH, 1)
```

```python
from contextlib import ExitStack

import numpy as np

import concourse.bass as bass
from concourse import mybir

F32 = mybir.dt.float32
F32R = mybir.dt.float32r
F16 = mybir.dt.float16
I32 = mybir.dt.int32
ALU = mybir.AluOpType
ACT = mybir.ActivationFunctionType

BATCH = 2048
D = 128
NF = 26
VOCAB = [125000, 1000, 1250, 1250, 12500, 1250, 12500, 1000, 12500, 12500, 1000, 12500, 1250,
         12500, 12500, 12500, 1250, 1000, 1250, 1250, 1000, 1250, 1000, 1250, 1250, 1250]
PICKED = [f for f in range(NF) if VOCAB[f] == min(VOCAB)]
NP = len(PICKED)
CH = 8
KR = min(VOCAB) // CH
GATHERED = [f for f in range(NF) if f not in PICKED]
NV = NF + 1
VECTORS = [NF] + GATHERED + PICKED
NR = 1 + len(GATHERED)
SLOT = 32
P = 128
TILES = BATCH // P
PAIRS_OF_TILES = TILES // 2
H1, H2 = 512, 256
M1, M2 = H1 // P, H2 // P

SHIFTS = NV // 2
NPAIR = NV * SHIFTS
KT = 3
ROWS = NV // KT
KP = ROWS * SHIFTS
WIDE = NV + SHIFTS

GROUP = 4
NG = (NR + GROUP - 1) // GROUP
GROUPS = [list(range(g * GROUP, min(g * GROUP + GROUP, NR))) for g in range(NG)]
GATHERS = [sum(s > 0 for s in slots) for slots in GROUPS]
LOOKS = NP // 2
TBANKS = 3

PASSAGE = ([x for k in range(LOOKS) for x in (("look", 0, k), ("turn", 0, k))]
           + [("turn", 0, g) for g in range(LOOKS, NG)] + [("turn", 1, g) for g in range(NG)])
MOVER = [x[0] == "look" or (x[1] == 0 and x[2] % 2 == 1 and x[2] >= LOOKS) or (x[1] == 1 and x[2] % 2 == 0)
         for x in PASSAGE]
assert len(PASSAGE) % TBANKS == 0
EARLY = [[0, 1, 2, 3], [9, 10, 11]]
LATE = [[4, 5, 6, 7, 8], [12, 13, 14]]
AHEAD = [[0, 1], [2]]
GRAM_BANKS = 2
QUADS = 4
PER_QUAD = P // QUADS
PER_BANK = PER_QUAD // GRAM_BANKS


def pair_rows():
    rows = []
    for i in range(NV):
        for t in range(1, SHIFTS + 1):
            a, b = sorted((VECTORS[i], VECTORS[(i + t) % NV]))
            if b == NF:
                rows.append(D + a)
            else:
                rows.append(D + NF + a * NF - a * (a + 1) // 2 + b - a - 1)
    return rows


def build(nc, dense, ids, ids_picked, tables, w1_pairs, w1_dense, b1, w2, b2, w3, out):
    with ExitStack() as ctx:
        def sb(name, shape, dt=F32):
            return ctx.enter_context(nc.sbuf_tensor(name, shape, dt))

        def sem(name):
            return ctx.enter_context(nc.semaphore(name))

        ident = sb("ident", [P, P])
        w1p = sb("w1p", [KP, KT, H1])
        w1d = sb("w1d", [D, 2, H1])
        w1x = sb("w1x", [D, H1])
        w2s = sb("w2s", [P, M1, H2])
        w3s = sb("w3s", [P, M2])
        b1s = sb("b1s", [P, M1])
        b2s = sb("b2s", [P, M2])
        idx = [sb(f"idx{q}", [P, NF], I32) for q in range(2)]
        rows = [sb(f"rows{q}", [P, NR, D]) for q in range(2)]
        emb = [sb(f"emb{q}", [D, P, SLOT]) for q in range(2)]
        xT = [sb(f"xT{q}", [D, P]) for q in range(2)]
        raw = [sb(f"raw{j}", [KR, CH, D]) for j in range(2)]
        high = [sb(f"high{f}", [KR, CH, D], F32R) for f in range(NP)]
        low = [sb(f"low{f}", [KR, CH, D], F32R) for f in range(NP)]
        row_i = sb("row_i", [KR, CH], I32)
        row_f = sb("row_f", [KR, CH])
        ids_int = sb("ids_int", [P, PAIRS_OF_TILES * 2 * NP], I32)
        ids_col = sb("ids_col", [P, 2, NP], F16)
        ident_h = sb("ident_h", [P, P], F16)
        hot = [sb(f"hot{f}", [KR, CH, 2 * P], F32R) for f in range(NP)]
        gram = sb("gram", [P, SLOT, WIDE])
        packed = sb("packed", [P, NPAIR])
        feat = sb("feat", [KP, KT, P])
        h1 = sb("h1", [P, M1, P])
        h2 = sb("h2", [P, M2, P])
        y_sb = sb("y_sb", [1, P])

        psT = [ctx.enter_context(nc.psum_tensor(f"psT{b}", [P, GROUP, P], F32)) for b in range(TBANKS)]
        psG = ctx.enter_context(nc.psum_tensor("psG", [P, GRAM_BANKS, 512], F32))
        psI = ctx.enter_context(nc.psum_tensor("psI", [P, 2, 2 * P], F32))
        psH1 = ctx.enter_context(nc.psum_tensor("psH1", [P, M1, P], F32))
        psF = ctx.enter_context(nc.psum_tensor("psF", [P, 4, P], F32))
        psH2 = psF
        psY = psF[0:1, KT, :]

        consts_loaded = sem("consts_loaded")
        picks_loaded = sem("picks_loaded")
        ident_zeroed = sem("ident_zeroed")
        ident_ready = sem("ident_ready")
        pads_zeroed = sem("pads_zeroed")
        w1x_ready = sem("w1x_ready")
        ids_loaded = [sem(f"ids_loaded{q}") for q in range(2)]
        dense_loaded = [sem(f"dense_loaded{q}") for q in range(2)]
        gathered = [[sem(f"gathered{q}_{g}") for g in range(NG)] for q in range(2)]
        raw_loaded = [sem(f"raw_loaded{j}") for j in range(2)]
        high_ready = sem("high_ready")
        low_ready = sem("low_ready")
        ident_h_ready = sem("ident_h_ready")
        rows_numbered = sem("rows_numbered")
        row_f_ready = sem("row_f_ready")
        ids_col_ready = sem("ids_col_ready")
        ids_spread = sem("ids_spread")
        hot_ready = sem("hot_ready")
        looked_up = sem("looked_up")
        transposed = sem("transposed")
        emb_by_act = sem("emb_by_act")
        emb_by_dve = sem("emb_by_dve")
        gram_done = sem("gram_done")
        gram_turned = sem("gram_turned")
        packed_ready = sem("packed_ready")
        feat_turned = sem("feat_turned")
        feat_ready = sem("feat_ready")
        l1_done = sem("l1_done")
        h1_ready = sem("h1_ready")
        l2_done = sem("l2_done")
        h2_ready = sem("h2_ready")
        l3_done = sem("l3_done")
        y_copied = sem("y_copied")
        y_stored = sem("y_stored")
        N_CONSTS = 6

        def moved(pair, n):
            ours = [m for m in range(len(PASSAGE)) if MOVER[m] == MOVER[n]]
            return (emb_by_act if MOVER[n] else emb_by_dve), len(ours) * pair + (ours.index(n) + 1)

        def bank_free(pair, n):
            return moved(pair, n - TBANKS) if n >= TBANKS else moved(pair - 1, n - TBANKS + len(PASSAGE))

        def before(pair, q):
            return (pair, 0) if q else (pair - 1, 1)

        block = ctx.enter_context(nc.Block())

        @block.sync
        def _(sp):
            def load(pair, q, fresh):
                if not fresh:
                    sp.wait_ge(transposed, 2 * NG * pair + (NG * q - NG))
                at = bass.ds((2 * pair + q) * P, P)
                sp.dma_start(idx[q][:, :], ids[at, :]).then_inc(ids_loaded[q], 16)
                sp.dma_start(rows[q][:, 0, :], dense[at, :]).then_inc(dense_loaded[q], 16)

            load(0, 0, True)
            load(0, 1, True)
            sp.dma_start(ids_int[:, :], ids_picked).then_inc(picks_loaded, 16)
            for k, f in enumerate(PICKED):
                if k >= 2:
                    sp.wait_ge(low_ready, k - 1)
                sp.dma_start(raw[k % 2][:, :, :], tables[f].rearrange("(p c) d -> p c d", c=CH)).then_inc(raw_loaded[k % 2], 16)
            with sp.Fori(1, PAIRS_OF_TILES) as pair:
                load(pair, 0, False)
                load(pair, 1, False)

        @block.gpsimd
        def _(pool):
            nc.gpsimd.memset(ident[:, :], 0.0).then_inc(ident_zeroed, 1)
            pool.wait_ge(ident_zeroed, 1)
            nc.gpsimd.affine_select(out=ident[:, :], in_=ident[:, :], compare_op=ALU.not_equal, fill=1.0,
                                    base=0, pattern=[[-1, P]], channel_multiplier=1).then_inc(ident_ready, 1)
            nc.gpsimd.iota(row_i[:, :], pattern=[[1, CH]], base=0, channel_multiplier=CH).then_inc(rows_numbered, 1)

            freed = pool.alloc_register("freed")

            def gather(pair, q, fresh):
                pool.wait_ge(ids_loaded[q], 16 * pair + 16)
                for g, slots in enumerate(GROUPS):
                    if not fresh:
                        pool.wait_ge(transposed, freed)
                        pool.reg_add(freed, freed, 1)
                    for s in slots:
                        if s > 0:
                            f = VECTORS[s]
                            pool.indirect_dma_start(
                                out=rows[q][:, s, :], out_offset=None, in_=tables[f],
                                in_offset=bass.IndirectOffsetOnAxis(ap=idx[q][:, f:f + 1], axis=0),
                            ).then_inc(gathered[q][g], 16)

            gather(0, 0, True)
            gather(0, 1, True)
            pool.reg_mov(freed, 1)
            with pool.Fori(1, PAIRS_OF_TILES) as pair:
                gather(pair, 0, False)
                gather(pair, 1, False)

        def emb_free(eng, pair, q):
            eng.wait_ge(gram_done, 2 * pair + (q - 1))

        def move(eng, copy, pair, q, n, fresh):
            kind, _, g = PASSAGE[n]
            bank = psT[n % TBANKS]
            if kind == "look":
                eng.wait_ge(looked_up, LOOKS * pair + (g + 1))
                if not fresh:
                    emb_free(eng, pair, 1)
                slots = slice(NR + 2 * g, NR + 2 * g + 2)
                for t in range(2):
                    last = copy(emb[t][:, :, slots], bank[:, :, :].rearrange(
                        "d (s t) b -> d t b s", t=2)[:, t, :, :])
                return last
            eng.wait_ge(transposed, 2 * NG * pair + (NG * q + g + 1))
            if not fresh:
                emb_free(eng, pair, q)
            slots = GROUPS[g]
            last = copy(emb[q][:, :, slots[0]:slots[-1] + 1],
                        bank[:, 0:len(slots), :].rearrange("d s b -> d b s"))
            if g == 0:
                if not fresh:
                    eng.wait_ge(l1_done, 2 * pair + (q - 1))
                last = copy(xT[q][:, :], bank[:, 0, :])
            return last

        @block.scalar
        def _(act):
            act.dma_start(w1p[:, :, :], w1_pairs).then_inc(consts_loaded, 16)
            act.dma_start(w1d[:, :, :], w1_dense).then_inc(consts_loaded, 16)
            act.dma_start(b1s[:, :], b1).then_inc(consts_loaded, 16)
            act.dma_start(w2s[:, :, :], w2).then_inc(consts_loaded, 16)
            act.dma_start(b2s[:, :], b2).then_inc(consts_loaded, 16)
            act.dma_start(w3s[:, :], w3).then_inc(consts_loaded, 16)

            def fill(pair, q, fresh):
                for n, x in enumerate(PASSAGE):
                    if x[1] == q and MOVER[n]:
                        move(act, nc.scalar.copy, pair, q, n, fresh).then_inc(emb_by_act, 1)

            def head(pair, q, fresh):
                act.wait_ge(l1_done, 2 * pair + (q + 1))
                act.wait_ge(l2_done, 2 * pair + q)
                for m in range(M1):
                    nc.scalar.activation(h1[:, m, :], psH1[:, m, :], ACT.Relu,
                                         bias=b1s[:, m:m + 1]).then_inc(h1_ready, 1)
                act.wait_ge(l2_done, 2 * pair + (q + 1))
                act.wait_ge(l3_done, 2 * pair + q)
                for m in range(M2):
                    nc.scalar.activation(h2[:, m, :], psH2[:, m, :], ACT.Relu,
                                         bias=b2s[:, m:m + 1]).then_inc(h2_ready, 1)
                act.wait_ge(l3_done, 2 * pair + (q + 1))
                if not fresh:
                    act.wait_ge(y_stored, 32 * pair + 16 * q)
                nc.scalar.copy(y_sb[:, :], psY).then_inc(y_copied, 1)
                act.wait_ge(y_copied, 2 * pair + (q + 1))
                act.dma_start(out[:, bass.ds((2 * pair + q) * P, P)], y_sb[:, :]).then_inc(y_stored, 16)

            for k in range(NP):
                act.wait_ge(raw_loaded[k % 2], 16 * (k // 2 + 1))
                nc.scalar.copy(high[k][:, :, :], raw[k % 2][:, :, :]).then_inc(high_ready, 1)
            fill(0, 0, True)
            act.wait_ge(consts_loaded, 16 * N_CONSTS)
            fill(0, 1, True)
            head(0, 0, True)
            with act.Fori(1, PAIRS_OF_TILES) as pair:
                fill(pair, 0, False)
                head(pair - 1, 1, False)
                fill(pair, 1, False)
                head(pair, 0, False)
            head(PAIRS_OF_TILES - 1, 1, False)
            act.wait_ge(y_stored, 16 * TILES)

        @block.vector
        def _(dve):
            def fill(pair, ns, fresh):
                for n in ns:
                    if not MOVER[n]:
                        move(dve, nc.vector.tensor_copy, pair, PASSAGE[n][1], n, fresh).then_inc(emb_by_dve, 1)

            def take_ids(pair, fresh):
                if not fresh:
                    dve.wait_ge(ids_spread, LOOKS * pair)
                nc.vector.tensor_copy(ids_col[:, :, :].rearrange("p t k -> p (t k)"),
                                      ids_int[:, bass.ds(2 * NP * pair, 2 * NP)]).then_inc(ids_col_ready, 1)

            def mark(pair, g, fresh):
                dve.wait_ge(ids_spread, LOOKS * pair + (g + 1))
                if not fresh:
                    dve.wait_ge(looked_up, LOOKS * pair + (g + 1 - LOOKS))
                for k in (2 * g, 2 * g + 1):
                    nc.vector.tensor_tensor(
                        hot[k][:, :, :], psI[0:KR, k % 2, :].unsqueeze(1).broadcast_to([KR, CH, 2 * P]),
                        row_f[:, :].unsqueeze(2).broadcast_to([KR, CH, 2 * P]), ALU.is_equal,
                    ).then_inc(hot_ready, 1)

            def take_features(pair, q):
                dve.wait_ge(feat_turned, 2 * pair + (q + 1))
                dve.wait_ge(l1_done, 2 * pair + q)
                nc.vector.tensor_copy(feat[:, :, :], psF[0:KP, 0:KT, :]).then_inc(feat_ready, 1)

            def turn_gram(pair, q):
                dve.wait_ge(gram_done, 2 * pair + (q + 1))
                dve.wait_ge(packed_ready, 2 * pair + q)
                for lo, n in ((0, NV), (NV, SHIFTS)):
                    src = psG[:, :, 0:PER_BANK * NV].rearrange("p k (g j) -> p j k g", j=NV)[:, 0:n, :, :]
                    dst = gram[:, :, lo:lo + n].rearrange("p i j -> p j i")
                    nc.vector.transpose(dst, src).then_inc(gram_turned, 1)
                dve.wait_ge(gram_turned, 4 * pair + (2 * q + 2))
                dve.wait_ge(feat_turned, 2 * pair + q)
                src = gram[:, :, :].rearrange("p i j -> p (i j)")[:, 1:NV * (WIDE + 1) + 1]
                src = src.rearrange("p (i j) -> p i j", j=WIDE + 1)[:, :, 0:SHIFTS]
                dst = packed[:, :].rearrange("p (i t) -> p i t", t=SHIFTS)
                nc.vector.tensor_copy(dst, src).then_inc(packed_ready, 1)

            for q in range(2):
                nc.vector.memset(emb[q][:, :, NV:SLOT], 0.0).then_inc(pads_zeroed, 1)
            dve.wait_ge(ident_ready, 1)
            nc.vector.tensor_copy(ident_h[:, :], ident[:, :]).then_inc(ident_h_ready, 1)
            dve.wait_ge(rows_numbered, 1)
            nc.vector.tensor_copy(row_f[:, :], row_i[:, :]).then_inc(row_f_ready, 1)
            dve.wait_ge(row_f_ready, 1)
            dve.wait_ge(picks_loaded, 16)
            take_ids(0, True)
            for k in range(NP):
                if k % 2 == 0:
                    mark(0, k // 2, True)
                dve.wait_ge(high_ready, k + 1)
                nc.vector.tensor_tensor(low[k][:, :, :], raw[k % 2][:, :, :], high[k][:, :, :].bitcast(F32),
                                        ALU.subtract).then_inc(low_ready, 1)
            dve.wait_ge(consts_loaded, 16 * N_CONSTS)
            nc.vector.tensor_tensor(w1x[:, :], w1d[:, 0, :], w1d[:, 1, :], ALU.add).then_inc(w1x_ready, 1)

            def step(pair, q, fresh, more):
                fill(pair, EARLY[q], fresh)
                take_features(*before(pair, q))
                fill(pair, LATE[q], fresh)
                if more:
                    if q == 0:
                        take_ids(pair + 1, False)
                    for g in AHEAD[q]:
                        mark(pair + 1, g, False)
                turn_gram(pair, q)

            fill(0, EARLY[0] + LATE[0], True)
            take_ids(1, False)
            for g in AHEAD[0]:
                mark(1, g, False)
            turn_gram(0, 0)
            step(0, 1, True, True)
            with dve.Fori(1, PAIRS_OF_TILES - 1) as pair:
                step(pair, 0, False, True)
                step(pair, 1, False, True)
            step(PAIRS_OF_TILES - 1, 0, False, False)
            step(PAIRS_OF_TILES - 1, 1, False, False)
            take_features(PAIRS_OF_TILES - 1, 1)

        @block.tensor
        def _(pe):
            def spread(pair, g, fresh):
                pe.wait_ge(ids_col_ready, pair + 1)
                if not fresh or g > 0:
                    pe.wait_ge(hot_ready, NP * pair + 2 * g)
                for j in range(2):
                    for t in range(2):
                        last = nc.tensor.matmul(psI[0:KR, j, t * P:(t + 1) * P],
                                                ids_col[:, t, 2 * g + j:2 * g + j + 1].broadcast_to([P, KR]),
                                                ident_h[:, :], start=True, stop=True)
                last.then_inc(ids_spread, 1)

            def bank_taken(pair, n, fresh):
                if not fresh or n >= TBANKS:
                    pe.wait_ge(*bank_free(pair, n))

            def look(pair, n, fresh):
                g = PASSAGE[n][2]
                pe.wait_ge(hot_ready, NP * pair + (2 * g + 2))
                bank_taken(pair, n, fresh)
                for j in range(2):
                    k = 2 * g + j
                    if fresh:
                        pe.wait_ge(low_ready, k + 1)
                    parts = [(part, c) for part in (high[k], low[k]) for c in range(CH)]
                    for m, (part, c) in enumerate(parts):
                        last = nc.tensor.matmul(psT[n % TBANKS][:, 2 * j:2 * j + 2, :], part[:, c, :], hot[k][:, c, :],
                                                start=(m == 0), stop=(m == len(parts) - 1))
                last.then_inc(looked_up, 1)

            def turn(pair, n, fresh):
                _, q, g = PASSAGE[n]
                pe.wait_ge(gathered[q][g], (16 * GATHERS[g]) * pair + 16 * GATHERS[g])
                if g == 0:
                    pe.wait_ge(dense_loaded[q], 16 * pair + 16)
                bank_taken(pair, n, fresh)
                for j, s in enumerate(GROUPS[g]):
                    last = nc.tensor.transpose(psT[n % TBANKS][:, j, :], rows[q][:, s, :], ident[:, :])
                last.then_inc(transposed, 1)

            def pass_on(pair, ns, fresh):
                for n in ns:
                    (look if PASSAGE[n][0] == "look" else turn)(pair, n, fresh)

            def products(pair, q, bank):
                if bank == 0:
                    final = LATE[q][-1]
                    pe.wait_ge(*moved(pair, final))
                    pe.wait_ge(*moved(pair, max(n for n in range(final) if MOVER[n] != MOVER[final])))
                    pe.wait_ge(gram_turned, 4 * pair + 2 * q)
                for g in range(PER_BANK):
                    for c in range(QUADS):
                        b = c * PER_QUAD + bank * PER_BANK + g
                        last = nc.tensor.matmul(
                            psG[c * SLOT:(c + 1) * SLOT, bank, g * NV:(g + 1) * NV],
                            emb[q][:, b, :], emb[q][:, b, 0:NV], start=True, stop=True)
                if bank == GRAM_BANKS - 1:
                    last.then_inc(gram_done, 1)

            def turn_features(pair, q):
                pe.wait_ge(packed_ready, 2 * pair + (q + 1))
                pe.wait_ge(y_copied, 2 * pair + q)
                for k in range(KT):
                    last = nc.tensor.transpose(psF[0:KP, k, :], packed[:, k * KP:(k + 1) * KP], ident[:, :])
                last.then_inc(feat_turned, 1)

            def layer1(pair, q):
                pe.wait_ge(feat_ready, 2 * pair + (q + 1))
                pe.wait_ge(h1_ready, (2 * M1) * pair + M1 * q)
                for m in range(M1):
                    cols = slice(m * P, (m + 1) * P)
                    nc.tensor.matmul(psH1[:, m, :], w1x[:, cols], xT[q][:, :], start=True, stop=False)
                    for k in range(KT):
                        last = nc.tensor.matmul(psH1[:, m, :], w1p[:, k, cols], feat[:, k, :],
                                                start=False, stop=(k == KT - 1))
                last.then_inc(l1_done, 1)

            def layer2(pair, q):
                pe.wait_ge(h1_ready, (2 * M1) * pair + (M1 * q + M1))
                for m in range(M2):
                    for k in range(M1):
                        last = nc.tensor.matmul(psH2[:, m, :], w2s[:, k, m * P:(m + 1) * P], h1[:, k, :],
                                                start=(k == 0), stop=(k == M1 - 1))
                last.then_inc(l2_done, 1)

            def layer3(pair, q):
                pe.wait_ge(h2_ready, (2 * M2) * pair + (M2 * q + M2))
                for k in range(M2):
                    last = nc.tensor.matmul(psY, w3s[:, k:k + 1], h2[:, k, :],
                                            start=(k == 0), stop=(k == M2 - 1))
                last.then_inc(l3_done, 1)

            def step(pair, q, fresh, more):
                done = before(pair, q)
                pass_on(pair, EARLY[q], fresh)
                turn_features(*done)
                pass_on(pair, LATE[q], fresh)
                layer1(*done)
                for bank in range(GRAM_BANKS):
                    if bank == 1:
                        layer2(*done)
                    if more and bank < len(AHEAD[q]):
                        spread(pair + 1, AHEAD[q][bank], False)
                    products(pair, q, bank)
                layer3(*done)

            pe.wait_ge(ident_h_ready, 1)
            for g in range(LOOKS):
                spread(0, g, True)
            pass_on(0, EARLY[0] + LATE[0], True)
            pe.wait_ge(pads_zeroed, 2)
            for bank in range(GRAM_BANKS):
                spread(1, AHEAD[0][bank], False)
                products(0, 0, bank)
            pe.wait_ge(consts_loaded, 16 * N_CONSTS)
            pe.wait_ge(w1x_ready, 1)
            step(0, 1, True, True)
            with pe.Fori(1, PAIRS_OF_TILES - 1) as pair:
                step(pair, 0, False, True)
                step(pair, 1, False, True)
            step(PAIRS_OF_TILES - 1, 0, False, False)
            step(PAIRS_OF_TILES - 1, 1, False, False)
            final = (PAIRS_OF_TILES - 1, 1)
            turn_features(*final)
            layer1(*final)
            layer2(*final)
            layer3(*final)


def kernel(**inputs):
    from concourse import bacc
    from concourse.bass_utils import run_bass_kernel_spmd

    w1 = np.asarray(inputs["W_top1"])
    w2 = np.asarray(inputs["W_top2"])
    w3 = np.asarray(inputs["W_top3"])
    arrays = {
        "dense": np.asarray(inputs["r_dense_features"]),
        "ids": np.asarray(inputs["ids"]),
        "w1_pairs": w1[pair_rows()].reshape(KT, KP, H1).transpose(1, 0, 2),
        "w1_dense": np.stack([w1[:D], w1[-D:]], axis=1),
        "b1": np.asarray(inputs["b_top1"]).reshape(M1, P).T,
        "w2": w2.reshape(M1, P, H2).transpose(1, 0, 2),
        "b2": np.asarray(inputs["b_top2"]).reshape(M2, P).T,
        "w3": w3.reshape(M2, P).T,
    }
    arrays["ids_picked"] = arrays["ids"][:, PICKED].reshape(TILES, P, NP).transpose(1, 0, 2).reshape(P, -1)
    for f in range(NF):
        arrays[f"tbl_{f}"] = np.asarray(inputs[f"tbl_{f}"])
    arrays = {k: np.ascontiguousarray(v) for k, v in arrays.items()}

    nc = bacc.Bacc("TRN2", target_bir_lowering=False, num_devices=1)
    arg = {k: nc.dram_tensor(k, v.shape, mybir.dt.from_np(v.dtype), kind="ExternalInput").ap()
           for k, v in arrays.items()}
    out = nc.dram_tensor("y", [1, BATCH], F32, kind="ExternalOutput").ap()
    build(nc, arg["dense"], arg["ids"], arg["ids_picked"], [arg[f"tbl_{f}"] for f in range(NF)], arg["w1_pairs"],
          arg["w1_dense"], arg["b1"], arg["w2"], arg["b2"], arg["w3"], out)
    r = run_bass_kernel_spmd(nc, [arrays], core_ids=[0])
    return r.results[0]["y"].reshape(BATCH, 1)
```

```python
from contextlib import ExitStack

import numpy as np

import concourse.bass as bass
from concourse import mybir

F32 = mybir.dt.float32
F32R = mybir.dt.float32r
F16 = mybir.dt.float16
I32 = mybir.dt.int32
ALU = mybir.AluOpType
ACT = mybir.ActivationFunctionType

BATCH = 2048
D = 128
NF = 26
VOCAB = [125000, 1000, 1250, 1250, 12500, 1250, 12500, 1000, 12500, 12500, 1000, 12500, 1250,
         12500, 12500, 12500, 1250, 1000, 1250, 1250, 1000, 1250, 1000, 1250, 1250, 1250]
NP = 7
PICKED = sorted(range(NF), key=lambda f: (VOCAB[f], f))[:NP]
KR = 125
CHS = [VOCAB[f] // KR for f in PICKED]
assert all(VOCAB[f] % KR == 0 and VOCAB[f] <= 2048 for f in PICKED)
GATHERED = [f for f in range(NF) if f not in PICKED]
NV = NF + 1
VECTORS = [NF] + GATHERED + PICKED
NR = 1 + len(GATHERED)
SLOT = 32
P = 128
TILES = BATCH // P
PAIRS_OF_TILES = TILES // 2
H1, H2 = 512, 256
M1, M2 = H1 // P, H2 // P

SHIFTS = NV // 2
NPAIR = NV * SHIFTS
KT = 3
ROWS = NV // KT
KP = ROWS * SHIFTS
WIDE = NV + SHIFTS

GROUP = 4
NG = (NR + GROUP - 1) // GROUP
GROUPS = [list(range(g * GROUP, min(g * GROUP + GROUP, NR))) for g in range(NG)]
GATHERS = [sum(s > 0 for s in slots) for slots in GROUPS]
LOOK = [list(range(k, min(k + 2, NP))) for k in range(0, NP, 2)]
LOOKS = len(LOOK)
LOOK_CH = max(sum(CHS[k] for k in ks) for ks in LOOK)
HOTS = 2
assert LOOKS % HOTS == 0
TBANKS = 3

STAGES = [[[("turn", 0), ("turn", 1)],
           [("turn", 2), ("turn", 3)],
           [("turn", 4)]],
          [[("look", 0), ("turn", 0)],
           [("turn", 1), ("turn", 2)],
           [("look", 1), ("turn", 3), ("look", 2), ("look", 3), ("turn", 4)]]]
LAST_STAGES = [[("turn", 0)], [("turn", 1), ("turn", 2)], [("turn", 3)], [("turn", 4)]]
FIRST = [("look", 0), ("turn", 0), ("turn", 1), ("look", 1), ("turn", 2), ("look", 2), ("look", 3),
         ("turn", 3), ("turn", 4)]
SPLIT_BEFORE = {("look", 0): [0, 1, 2, 3], ("turn", 0): [4], ("look", 1): [5], ("look", 2): [6]}
assert sum(SPLIT_BEFORE.values(), []) == list(range(NP))
RAWS = 3
PASSAGE = [(q, kind, g) for q in range(2) for stage in STAGES[q] for kind, g in stage]
BANK = {x: n % TBANKS for n, x in enumerate(PASSAGE)}
SPREAD_AT = {(0, "turn", 3): 0, (1, "turn", 0): 2, (1, "look", 2): 3}
SPREAD_IN_PRODUCTS = 1
GRAM_BANKS = 2
QUADS = 4
PER_QUAD = P // QUADS
PER_BANK = PER_QUAD // GRAM_BANKS


def pair_rows():
    rows = []
    for i in range(NV):
        for t in range(1, SHIFTS + 1):
            a, b = sorted((VECTORS[i], VECTORS[(i + t) % NV]))
            if b == NF:
                rows.append(D + a)
            else:
                rows.append(D + NF + a * NF - a * (a + 1) // 2 + b - a - 1)
    return rows


def build(nc, dense, ids, ids_picked, tables, w1_pairs, w1_dense, b1, w2, b2, w3, out):
    with ExitStack() as ctx:
        def sb(name, shape, dt=F32):
            return ctx.enter_context(nc.sbuf_tensor(name, shape, dt))

        def sem(name):
            return ctx.enter_context(nc.semaphore(name))

        ident = sb("ident", [P, P])
        w1p = sb("w1p", [KP, KT, H1])
        w1d = sb("w1d", [D, 2, H1])
        w1x = sb("w1x", [D, H1])
        w2s = sb("w2s", [P, M1, H2])
        w3s = sb("w3s", [P, M2])
        b1s = sb("b1s", [P, M1])
        b2s = sb("b2s", [P, M2])
        idx = [sb(f"idx{q}", [P, NF], I32) for q in range(2)]
        rows = [sb(f"rows{q}", [P, NR, D]) for q in range(2)]
        emb = [sb(f"emb{q}", [D, P, SLOT]) for q in range(2)]
        xT = [sb(f"xT{q}", [D, P]) for q in range(2)]
        raw = [sb(f"raw{j}", [KR, max(CHS), D]) for j in range(RAWS)]
        high = [sb(f"high{k}", [KR, CHS[k], D], F32R) for k in range(NP)]
        low = [sb(f"low{k}", [KR, CHS[k], D], F32R) for k in range(NP)]
        row_i = {ch: sb(f"row_i{ch}", [KR, ch], I32) for ch in sorted(set(CHS))}
        row_f = {ch: sb(f"row_f{ch}", [KR, ch]) for ch in sorted(set(CHS))}
        ids_int = sb("ids_int", [P, TILES * NP], I32)
        ids_h = sb("ids_h", [P, 2 * NP], F16)
        ident_h = sb("ident_h", [P, P], F16)
        hot = [sb(f"hot{r}", [KR, LOOK_CH, 2 * P], F32R) for r in range(HOTS)]
        side = sb("side", [D, NP, P])
        gram = sb("gram", [P, SLOT, WIDE])
        packed = sb("packed", [P, NPAIR])
        feat = sb("feat", [KP, KT, P])
        h1 = sb("h1", [P, M1, P])
        h2 = sb("h2", [P, M2, P])
        y_sb = sb("y_sb", [1, P])

        psT = [ctx.enter_context(nc.psum_tensor(f"psT{b}", [P, GROUP, P], F32)) for b in range(TBANKS)]
        psG = ctx.enter_context(nc.psum_tensor("psG", [P, GRAM_BANKS, 512], F32))
        psI = ctx.enter_context(nc.psum_tensor("psI", [P, 2, 2 * P], F32))
        psH1 = ctx.enter_context(nc.psum_tensor("psH1", [P, M1, P], F32))
        psF = ctx.enter_context(nc.psum_tensor("psF", [P, 4, P], F32))
        psH2 = psF
        psY = psF[0:1, KT, :]
        h1_whole = [psH1[:, m, :] for m in range(M1)]
        h1_halves = h1_whole[:M1 // 2] + [psT[2][:, m, :] for m in range(M1 // 2, M1)]
        psF_last = psT[0]

        consts_loaded = sem("consts_loaded")
        picks_loaded = sem("picks_loaded")
        ident_zeroed = sem("ident_zeroed")
        ident_ready = sem("ident_ready")
        pads_zeroed = sem("pads_zeroed")
        w1x_ready = sem("w1x_ready")
        ids_loaded = [sem(f"ids_loaded{q}") for q in range(2)]
        dense_loaded = [sem(f"dense_loaded{q}") for q in range(2)]
        gathered = [[sem(f"gathered{q}_{g}") for g in range(NG)] for q in range(2)]
        raw_loaded = [sem(f"raw_loaded{j}") for j in range(RAWS)]
        high_ready = sem("high_ready")
        low_ready = sem("low_ready")
        ident_h_ready = sem("ident_h_ready")
        rows_numbered = sem("rows_numbered")
        row_f_ready = sem("row_f_ready")
        ids_h_ready = sem("ids_h_ready")
        ids_spread = sem("ids_spread")
        hot_ready = sem("hot_ready")
        looked_up = sem("looked_up")
        transposed = sem("transposed")
        turn_moved = sem("turn_moved")
        look_moved = sem("look_moved")
        placed = sem("placed")
        gram_done = sem("gram_done")
        gram_turned = sem("gram_turned")
        packed_ready = sem("packed_ready")
        feat_turned = sem("feat_turned")
        feat_ready = sem("feat_ready")
        l1_done = sem("l1_done")
        l1_half_done = sem("l1_half_done")
        h1_ready = sem("h1_ready")
        l2_done = sem("l2_done")
        h2_ready = sem("h2_ready")
        l3_done = sem("l3_done")
        y_copied = sem("y_copied")
        y_stored = sem("y_stored")
        N_CONSTS = 6

        def is_pair(pair, n):
            return isinstance(pair, int) and pair == n

        def moved(pair, x):
            q, kind, g = x
            if kind == "look":
                return look_moved, LOOKS * pair + (LOOKS + g + 1)
            return turn_moved, 2 * NG * pair + (NG * q + g + 1)

        def previous(pair, x, looks):
            if is_pair(pair, 0):
                history = [((1, "look", g), -1) if kind == "look" else ((0, "turn", g), 0)
                           for kind, g in FIRST]
                if looks:
                    history += [(y, 0) for y in PASSAGE if y[0] == 1]
            else:
                history = [(y, pair - 1) for y in PASSAGE]
                history += [(y, pair) for y in PASSAGE if looks or y[1] == "turn"]
            at = max(n for n, (y, _) in enumerate(history) if y == x)
            for y, which in reversed(history[:at]):
                if BANK[y] == BANK[x]:
                    return moved(which, y)
            return None

        def before(pair, q):
            return (pair, 0) if q else (pair - 1, 1)

        block = ctx.enter_context(nc.Block())

        @block.sync
        def _(sp):
            def load(pair, q, fresh):
                if not fresh:
                    sp.wait_ge(transposed, 2 * NG * pair + (NG * q - NG))
                at = bass.ds((2 * pair + q) * P, P)
                sp.dma_start(idx[q][:, :], ids[at, :]).then_inc(ids_loaded[q], 16)
                sp.dma_start(rows[q][:, 0, :], dense[at, :]).then_inc(dense_loaded[q], 16)

            sp.dma_start(ids_int[:, :], ids_picked).then_inc(picks_loaded, 16)
            load(0, 0, True)
            for k, f in enumerate(PICKED):
                if k == 2:
                    load(0, 1, True)
                if k >= RAWS:
                    sp.wait_ge(low_ready, k + 1 - RAWS)
                sp.dma_start(raw[k % RAWS][:, 0:CHS[k], :],
                             tables[f].rearrange("(p c) d -> p c d", c=CHS[k])).then_inc(raw_loaded[k % RAWS], 16)
            sp.dma_start(w1d[:, :, :], w1_dense).then_inc(consts_loaded, 16)
            sp.dma_start(w1p[:, :, :], w1_pairs).then_inc(consts_loaded, 16)
            sp.dma_start(b1s[:, :], b1).then_inc(consts_loaded, 16)
            sp.dma_start(w2s[:, :, :], w2).then_inc(consts_loaded, 16)
            sp.dma_start(b2s[:, :], b2).then_inc(consts_loaded, 16)
            sp.dma_start(w3s[:, :], w3).then_inc(consts_loaded, 16)
            with sp.Fori(1, PAIRS_OF_TILES) as pair:
                load(pair, 0, False)
                load(pair, 1, False)

        @block.gpsimd
        def _(pool):
            nc.gpsimd.memset(ident[:, :], 0.0).then_inc(ident_zeroed, 1)
            pool.wait_ge(ident_zeroed, 1)
            nc.gpsimd.affine_select(out=ident[:, :], in_=ident[:, :], compare_op=ALU.not_equal, fill=1.0,
                                    base=0, pattern=[[-1, P]], channel_multiplier=1).then_inc(ident_ready, 1)
            for ch in row_i:
                nc.gpsimd.iota(row_i[ch][:, :], pattern=[[1, ch]], base=0,
                               channel_multiplier=ch).then_inc(rows_numbered, 1)

            freed = pool.alloc_register("freed")

            def gather(pair, q, fresh):
                pool.wait_ge(ids_loaded[q], 16 * pair + 16)
                for g, slots in enumerate(GROUPS):
                    if not fresh:
                        pool.wait_ge(transposed, freed)
                        pool.reg_add(freed, freed, 1)
                    for s in slots:
                        if s > 0:
                            f = VECTORS[s]
                            pool.indirect_dma_start(
                                out=rows[q][:, s, :], out_offset=None, in_=tables[f],
                                in_offset=bass.IndirectOffsetOnAxis(ap=idx[q][:, f:f + 1], axis=0),
                            ).then_inc(gathered[q][g], 16)

            gather(0, 0, True)
            gather(0, 1, True)
            pool.reg_mov(freed, 1)
            with pool.Fori(1, PAIRS_OF_TILES) as pair:
                gather(pair, 0, False)
                gather(pair, 1, False)

        @block.scalar
        def _(act):
            def emb_free(pair, q):
                act.wait_ge(gram_done, 2 * pair + (q - 1))

            def move_look(pair, g, fresh):
                bank = psT[BANK[1, "look", g]][:, :, :].rearrange("d (s t) b -> d t s b", t=2)
                act.wait_ge(looked_up, LOOKS * pair + (g + 1))
                if not fresh:
                    emb_free(pair, 0)
                    act.wait_ge(placed, pair)
                ks = LOOK[g]
                nc.scalar.copy(emb[0][:, :, NR + ks[0]:NR + ks[-1] + 1],
                               bank[:, 0, 0:len(ks), :].rearrange("d s b -> d b s"))
                nc.scalar.copy(side[:, ks[0]:ks[-1] + 1, :], bank[:, 1, 0:len(ks), :]).then_inc(look_moved, 1)

            def move_turn(pair, q, g, fresh):
                bank = psT[BANK[q, "turn", g]]
                act.wait_ge(transposed, 2 * NG * pair + (NG * q + g + 1))
                if not fresh:
                    emb_free(pair, q)
                slots = GROUPS[g]
                last = nc.scalar.copy(emb[q][:, :, slots[0]:slots[-1] + 1],
                                      bank[:, 0:len(slots), :].rearrange("d s b -> d b s"))
                if g == 0:
                    if not fresh:
                        act.wait_ge(l1_done, 2 * pair + (q - 1))
                    last = nc.scalar.copy(xT[q][:, :], bank[:, 0, :])
                last.then_inc(turn_moved, 1)

            def fill(pair, q, stage, fresh, looks):
                for kind, g in stage:
                    if kind == "turn":
                        move_turn(pair, q, g, fresh)
                    elif looks:
                        move_look(pair + 1, g, False)

            def take_features(pair, q, bank=psF):
                act.wait_ge(feat_turned, 2 * pair + (q + 1))
                act.wait_ge(l1_done, 2 * pair + q)
                nc.scalar.copy(feat[:, :, :], bank[0:KP, 0:KT, :]).then_inc(feat_ready, 1)

            def hidden1(pair, q, where=h1_whole):
                act.wait_ge(l2_done, 2 * pair + q)
                for m in range(M1):
                    if m == 0 and where is h1_halves:
                        act.wait_ge(l1_half_done, 1)
                    elif m == 0 or (m == M1 // 2 and where is h1_halves):
                        act.wait_ge(l1_done, 2 * pair + (q + 1))
                    nc.scalar.activation(h1[:, m, :], where[m], ACT.Relu,
                                         bias=b1s[:, m:m + 1]).then_inc(h1_ready, 1)

            def hidden2(pair, q):
                act.wait_ge(l2_done, 2 * pair + (q + 1))
                act.wait_ge(l3_done, 2 * pair + q)
                for m in range(M2):
                    nc.scalar.activation(h2[:, m, :], psH2[:, m, :], ACT.Relu,
                                         bias=b2s[:, m:m + 1]).then_inc(h2_ready, 1)

            def results(pair, q):
                act.wait_ge(l3_done, 2 * pair + (q + 1))
                if q == 1 or not is_pair(pair, 0):
                    act.wait_ge(y_stored, 32 * pair + 16 * q)
                nc.scalar.copy(y_sb[:, :], psY).then_inc(y_copied, 1)
                act.wait_ge(y_copied, 2 * pair + (q + 1))
                act.dma_start(out[:, bass.ds((2 * pair + q) * P, P)], y_sb[:, :]).then_inc(y_stored, 16)

            def step(pair, q, fresh, looks):
                fill(pair, q, STAGES[q][0], fresh, looks)
                if not fresh:
                    hidden2(pair - 1, q)
                fill(pair, q, STAGES[q][1], fresh, looks)
                if not fresh:
                    results(pair - 1, q)
                fill(pair, q, STAGES[q][2], fresh, looks)
                if not fresh or q == 1:
                    take_features(*before(pair, q))
                    hidden1(*before(pair, q))

            for kind, g in FIRST:
                for k in SPLIT_BEFORE.get((kind, g), []):
                    act.wait_ge(raw_loaded[k % RAWS], 16 * (k // RAWS + 1))
                    nc.scalar.copy(high[k][:, :, :], raw[k % RAWS][:, 0:CHS[k], :]).then_inc(high_ready, 1)
                if kind == "look":
                    move_look(0, g, True)
                else:
                    move_turn(0, 0, g, True)
            step(0, 1, True, True)
            step(1, 0, False, True)
            step(1, 1, False, True)
            with act.Fori(2, PAIRS_OF_TILES - 1) as pair:
                step(pair, 0, False, True)
                step(pair, 1, False, True)
            final = PAIRS_OF_TILES - 1
            step(final, 0, False, False)
            fill(final, 1, LAST_STAGES[0], False, False)
            hidden2(final - 1, 1)
            fill(final, 1, LAST_STAGES[1], False, False)
            results(final - 1, 1)
            fill(final, 1, LAST_STAGES[2], False, False)
            take_features(final, 0)
            fill(final, 1, LAST_STAGES[3], False, False)
            hidden1(final, 0)
            hidden2(final, 0)
            take_features(final, 1, psF_last)
            results(final, 0)
            hidden1(final, 1, h1_halves)
            hidden2(final, 1)
            results(final, 1)
            act.wait_ge(y_stored, 16 * TILES)

        @block.vector
        def _(dve):
            def take_ids(pair, fresh):
                if not fresh:
                    dve.wait_ge(ids_spread, LOOKS * pair)
                nc.vector.tensor_copy(ids_h[:, :],
                                      ids_int[:, bass.ds(2 * NP * pair, 2 * NP)]).then_inc(ids_h_ready, 1)

            def mark(pair, g, fresh):
                dve.wait_ge(ids_spread, LOOKS * pair + (g + 1))
                if not fresh or g >= HOTS:
                    dve.wait_ge(looked_up, LOOKS * pair + (g + 1 - HOTS))
                at = 0
                for j, k in enumerate(LOOK[g]):
                    ch = CHS[k]
                    last = nc.vector.tensor_tensor(
                        hot[g % HOTS][:, at:at + ch, :], psI[0:KR, j, :].unsqueeze(1).broadcast_to([KR, ch, 2 * P]),
                        row_f[ch][:, :].unsqueeze(2).broadcast_to([KR, ch, 2 * P]), ALU.is_equal)
                    at += ch
                last.then_inc(hot_ready, 1)

            def place(pair, fresh):
                dve.wait_ge(look_moved, LOOKS * pair + LOOKS)
                if not fresh:
                    dve.wait_ge(gram_done, 2 * pair)
                nc.vector.tensor_copy(emb[1][:, :, NR:NR + NP],
                                      side[:, :, :].rearrange("d s b -> d b s")).then_inc(placed, 1)

            def turn_gram(pair, q):
                dve.wait_ge(gram_done, 2 * pair + (q + 1))
                dve.wait_ge(packed_ready, 2 * pair + q)
                for lo, n in ((0, NV), (NV, SHIFTS)):
                    src = psG[:, :, 0:PER_BANK * NV].rearrange("p k (g j) -> p j k g", j=NV)[:, 0:n, :, :]
                    dst = gram[:, :, lo:lo + n].rearrange("p i j -> p j i")
                    nc.vector.transpose(dst, src).then_inc(gram_turned, 1)
                dve.wait_ge(gram_turned, 4 * pair + (2 * q + 2))
                dve.wait_ge(feat_turned, 2 * pair + q)
                src = gram[:, :, :].rearrange("p i j -> p (i j)")[:, 1:NV * (WIDE + 1) + 1]
                src = src.rearrange("p (i j) -> p i j", j=WIDE + 1)[:, :, 0:SHIFTS]
                dst = packed[:, :].rearrange("p (i t) -> p i t", t=SHIFTS)
                nc.vector.tensor_copy(dst, src).then_inc(packed_ready, 1)

            for q in range(2):
                nc.vector.memset(emb[q][:, :, NV:SLOT], 0.0).then_inc(pads_zeroed, 1)
            dve.wait_ge(ident_ready, 1)
            nc.vector.tensor_copy(ident_h[:, :], ident[:, :]).then_inc(ident_h_ready, 1)
            dve.wait_ge(rows_numbered, len(row_i))
            for ch in row_i:
                nc.vector.tensor_copy(row_f[ch][:, :], row_i[ch][:, :]).then_inc(row_f_ready, 1)
            dve.wait_ge(row_f_ready, len(row_i))
            dve.wait_ge(picks_loaded, 16)
            take_ids(0, True)
            for g in range(LOOKS):
                mark(0, g, True)
                for k in LOOK[g]:
                    dve.wait_ge(high_ready, k + 1)
                    nc.vector.tensor_tensor(low[k][:, :, :], raw[k % RAWS][:, 0:CHS[k], :],
                                            high[k][:, :, :].bitcast(F32), ALU.subtract).then_inc(low_ready, 1)

            def step(pair, q, fresh, looks):
                if looks and q == 0:
                    take_ids(pair + 1, False)
                if q == 0:
                    place(pair, fresh)
                for x in PASSAGE:
                    if looks and x[0] == q and x in SPREAD_AT:
                        mark(pair + 1, SPREAD_AT[x], False)
                if looks and q == 0 and not fresh:
                    mark(pair + 1, SPREAD_IN_PRODUCTS, False)
                turn_gram(pair, q)

            step(0, 0, True, True)
            mark(1, SPREAD_IN_PRODUCTS, False)
            dve.wait_ge(consts_loaded, 16 * N_CONSTS)
            nc.vector.tensor_tensor(w1x[:, :], w1d[:, 0, :], w1d[:, 1, :], ALU.add).then_inc(w1x_ready, 1)
            step(0, 1, True, True)
            with dve.Fori(1, PAIRS_OF_TILES - 1) as pair:
                step(pair, 0, False, True)
                step(pair, 1, False, True)
            step(PAIRS_OF_TILES - 1, 0, False, False)
            step(PAIRS_OF_TILES - 1, 1, False, False)

        @block.tensor
        def _(pe):
            def spread(pair, g, fresh):
                if g == 0:
                    pe.wait_ge(ids_h_ready, pair + 1)
                if not fresh or g > 0:
                    pe.wait_ge(hot_ready, LOOKS * pair + g)
                for j, k in enumerate(LOOK[g]):
                    for t in range(2):
                        at = NP * t + k
                        last = nc.tensor.matmul(psI[0:KR, j, t * P:(t + 1) * P],
                                                ids_h[:, at:at + 1].broadcast_to([P, KR]),
                                                ident_h[:, :], start=True, stop=True)
                last.then_inc(ids_spread, 1)

            def look(pair, g, fresh):
                pe.wait_ge(hot_ready, LOOKS * pair + (g + 1))
                at = 0
                for j, k in enumerate(LOOK[g]):
                    if fresh:
                        pe.wait_ge(low_ready, k + 1)
                    parts = [(part, c) for part in (high[k], low[k]) for c in range(CHS[k])]
                    for m, (part, c) in enumerate(parts):
                        last = nc.tensor.matmul(psT[BANK[1, "look", g]][:, 2 * j:2 * j + 2, :], part[:, c, :],
                                                hot[g % HOTS][:, at + c, :],
                                                start=(m == 0), stop=(m == len(parts) - 1))
                    at += CHS[k]
                last.then_inc(looked_up, 1)

            def turn(pair, q, g):
                pe.wait_ge(gathered[q][g], (16 * GATHERS[g]) * pair + 16 * GATHERS[g])
                if g == 0:
                    pe.wait_ge(dense_loaded[q], 16 * pair + 16)
                for j, s in enumerate(GROUPS[g]):
                    last = nc.tensor.transpose(psT[BANK[q, "turn", g]][:, j, :], rows[q][:, s, :], ident[:, :])
                last.then_inc(transposed, 1)

            def pass_on(pair, q, stage, looks):
                for kind, g in stage:
                    x = (q, kind, g)
                    if looks and x in SPREAD_AT:
                        spread(pair + 1, SPREAD_AT[x], False)
                    if (kind == "turn" or looks) and previous(pair, x, looks) is not None:
                        pe.wait_ge(*previous(pair, x, looks))
                    if kind == "turn":
                        turn(pair, q, g)
                    elif looks:
                        look(pair + 1, g, False)

            def products(pair, q, bank):
                if bank == 0:
                    pe.wait_ge(*moved(pair, (q, "turn", NG - 1)))
                    if q == 0:
                        pe.wait_ge(look_moved, LOOKS * pair + LOOKS)
                    else:
                        pe.wait_ge(placed, pair + 1)
                    pe.wait_ge(gram_turned, 4 * pair + 2 * q)
                for g in range(PER_BANK):
                    for c in range(QUADS):
                        b = c * PER_QUAD + bank * PER_BANK + g
                        last = nc.tensor.matmul(
                            psG[c * SLOT:(c + 1) * SLOT, bank, g * NV:(g + 1) * NV],
                            emb[q][:, b, :], emb[q][:, b, 0:NV], start=True, stop=True)
                if bank == GRAM_BANKS - 1:
                    last.then_inc(gram_done, 1)

            def turn_features(pair, q, bank=psF):
                pe.wait_ge(packed_ready, 2 * pair + (q + 1))
                if bank is psF:
                    pe.wait_ge(y_copied, 2 * pair + q)
                for k in range(KT):
                    last = nc.tensor.transpose(bank[0:KP, k, :], packed[:, k * KP:(k + 1) * KP], ident[:, :])
                last.then_inc(feat_turned, 1)

            def layer1_dense(pair, q, where=h1_whole):
                pe.wait_ge(h1_ready, (2 * M1) * pair + M1 * q)
                for m in range(M1):
                    nc.tensor.matmul(where[m], w1x[:, m * P:(m + 1) * P], xT[q][:, :], stop=False,
                                     start=(m == 0 or (m == M1 // 2 and where is h1_halves)))

            def layer1(pair, q, ms=range(M1), where=h1_whole, done=l1_done):
                if ms[0] == 0:
                    pe.wait_ge(feat_ready, 2 * pair + (q + 1))
                for m in ms:
                    for k in range(KT):
                        last = nc.tensor.matmul(where[m], w1p[:, k, m * P:(m + 1) * P], feat[:, k, :], start=False,
                                                stop=(done is not None and m == ms[-1] and k == KT - 1))
                if done is not None:
                    last.then_inc(done, 1)

            def layer2(pair, q):
                for m in range(M2):
                    for k in range(M1):
                        if m == 0:
                            pe.wait_ge(h1_ready, (2 * M1) * pair + (M1 * q + (k + 1)))
                        last = nc.tensor.matmul(psH2[:, m, :], w2s[:, k, m * P:(m + 1) * P], h1[:, k, :],
                                                start=(k == 0), stop=(k == M1 - 1))
                last.then_inc(l2_done, 1)

            def layer3(pair, q):
                pe.wait_ge(h2_ready, (2 * M2) * pair + (M2 * q + M2))
                for k in range(M2):
                    last = nc.tensor.matmul(psY, w3s[:, k:k + 1], h2[:, k, :],
                                            start=(k == 0), stop=(k == M2 - 1))
                last.then_inc(l3_done, 1)

            def step(pair, q, fresh, looks):
                pass_on(pair, q, STAGES[q][0], looks)
                if not fresh:
                    layer2(pair - 1, q)
                pass_on(pair, q, STAGES[q][1], looks)
                if not fresh:
                    layer3(pair - 1, q)
                pass_on(pair, q, STAGES[q][2], looks)
                if fresh and q == 1:
                    pe.wait_ge(consts_loaded, 16 * N_CONSTS)
                    pe.wait_ge(w1x_ready, 1)
                if not fresh or q == 1:
                    layer1_dense(*before(pair, q))
                    turn_features(*before(pair, q))
                products(pair, q, 0)
                if not fresh or q == 1:
                    layer1(*before(pair, q))
                if looks and q == 0:
                    spread(pair + 1, SPREAD_IN_PRODUCTS, False)
                products(pair, q, 1)

            pe.wait_ge(ident_h_ready, 1)
            spread(0, 0, True)
            for kind, g in FIRST:
                if kind == "look" and g < LOOKS - 1:
                    spread(0, g + 1, True)
                x = (1 if kind == "look" else 0, kind, g)
                if previous(0, x, False) is not None:
                    pe.wait_ge(*previous(0, x, False))
                if kind == "look":
                    look(0, g, True)
                else:
                    turn(0, 0, g)
            spread(1, 0, False)
            pe.wait_ge(pads_zeroed, 2)
            products(0, 0, 0)
            products(0, 0, 1)
            spread(1, 1, False)
            step(0, 1, True, True)
            with pe.Fori(1, PAIRS_OF_TILES - 1) as pair:
                step(pair, 0, False, True)
                step(pair, 1, False, True)
            final = PAIRS_OF_TILES - 1
            step(final, 0, False, False)
            pass_on(final, 1, LAST_STAGES[0], False)
            layer2(final - 1, 1)
            pass_on(final, 1, LAST_STAGES[1], False)
            layer3(final - 1, 1)
            pass_on(final, 1, LAST_STAGES[2], False)
            turn_features(final, 0)
            layer1_dense(final, 0)
            layer1(final, 0, range(0, M1 // 2), done=None)
            pass_on(final, 1, LAST_STAGES[3], False)
            layer1(final, 0, range(M1 // 2, M1))
            products(final, 1, 0)
            products(final, 1, 1)
            layer2(final, 0)
            layer1_dense(final, 1, h1_halves)
            turn_features(final, 1, psF_last)
            layer3(final, 0)
            layer1(final, 1, range(0, M1 // 2), h1_halves, l1_half_done)
            layer1(final, 1, range(M1 // 2, M1), h1_halves)
            pe.wait_ge(y_copied, TILES - 1)
            layer2(final, 1)
            layer3(final, 1)


def kernel(**inputs):
    from concourse import bacc
    from concourse.bass_utils import run_bass_kernel_spmd

    w1 = np.asarray(inputs["W_top1"])
    w2 = np.asarray(inputs["W_top2"])
    w3 = np.asarray(inputs["W_top3"])
    arrays = {
        "dense": np.asarray(inputs["r_dense_features"]),
        "ids": np.asarray(inputs["ids"]),
        "w1_pairs": w1[pair_rows()].reshape(KT, KP, H1).transpose(1, 0, 2),
        "w1_dense": np.stack([w1[:D], w1[-D:]], axis=1),
        "b1": np.asarray(inputs["b_top1"]).reshape(M1, P).T,
        "w2": w2.reshape(M1, P, H2).transpose(1, 0, 2),
        "b2": np.asarray(inputs["b_top2"]).reshape(M2, P).T,
        "w3": w3.reshape(M2, P).T,
    }
    arrays["ids_picked"] = arrays["ids"][:, PICKED].reshape(TILES, P, NP).transpose(1, 0, 2).reshape(P, -1)
    for f in range(NF):
        arrays[f"tbl_{f}"] = np.asarray(inputs[f"tbl_{f}"])
    arrays = {k: np.ascontiguousarray(v) for k, v in arrays.items()}

    nc = bacc.Bacc("TRN2", target_bir_lowering=False, num_devices=1)
    arg = {k: nc.dram_tensor(k, v.shape, mybir.dt.from_np(v.dtype), kind="ExternalInput").ap()
           for k, v in arrays.items()}
    out = nc.dram_tensor("y", [1, BATCH], F32, kind="ExternalOutput").ap()
    build(nc, arg["dense"], arg["ids"], arg["ids_picked"], [arg[f"tbl_{f}"] for f in range(NF)], arg["w1_pairs"],
          arg["w1_dense"], arg["b1"], arg["w2"], arg["b2"], arg["w3"], out)
    r = run_bass_kernel_spmd(nc, [arrays], core_ids=[0])
    return r.results[0]["y"].reshape(BATCH, 1)
```
